# Optimizing a Trainium2 kernel written in Bass

```python
import numpy as np
import jax
import jax.numpy as jnp

def _softmax(x, axis=-1):
    return jax.nn.softmax(x, axis=axis)

def _gelu(x):
    return jax.nn.gelu(x, approximate=True)

def _silu(x):
    return jax.nn.silu(x)

def _sigmoid(x):
    return jax.nn.sigmoid(x)

def _layernorm(x, axis=-1, eps=1e-05):
    m = jnp.mean(x, axis=axis, keepdims=True)
    v = jnp.var(x, axis=axis, keepdims=True)
    return (x - m) / jnp.sqrt(v + eps)

def _scatter_add(tgt, idx, src, axis=0):
    return tgt.at[idx].add(src)

def _segment_sum(src, seg, n):
    return jax.ops.segment_sum(src, seg, n)
kernel_name = 'mk_xattn_ffn_d2_seqx_r8_d45f6f'

def setup_inputs(seed: int=0):
    np.random.seed(seed)
    _w = jnp.asarray

    def _rec_inputs():
        import jax
        import jax.numpy as jnp
        _rk = jax.random.key(seed)
        x = -0.000125 + 0.9999 * jax.random.normal(jax.random.fold_in(_rk, 1), (8, 128, 256), jnp.float32)
        _lenS = 128 - jax.random.randint(jax.random.fold_in(_rk, 7), (8,), 0, max(1, 128 // 4) + 1, jnp.int32)
        _lenS2 = 128 - jax.random.randint(jax.random.fold_in(_rk, 8), (8,), 0, max(1, 128 // 4) + 1, jnp.int32)
        _ctx_2048P = jax.random.normal(jax.random.fold_in(_rk, 11), (8, 16, 256), jnp.float32)
        _ctx_2048c = jax.random.dirichlet(jax.random.fold_in(_rk, 511), 0.3 * jnp.ones((16,), jnp.float32), (8, 128))
        _ctx_2048t = jnp.einsum('bsk,bkd->bsd', _ctx_2048c, _ctx_2048P)
        _ctx_2048t = _ctx_2048t * jax.lax.rsqrt(jnp.mean(jnp.square(_ctx_2048t)) + 1e-12) * 0.953939
        ctx_2048 = -0.000514642 + 1.00011 * (_ctx_2048t + 0.3 * jax.random.normal(jax.random.fold_in(_rk, 611), (8, 128, 256), jnp.float32))
        _validS = jnp.arange(128)[None, :] < _lenS[:, None]
        _validS2 = jnp.arange(128)[None, :] < _lenS2[:, None]
        _causal = jnp.tril(jnp.ones((128, 128), dtype=bool))
        mask_BxS2_bk0 = jnp.logical_not(jnp.broadcast_to(_validS2[:, :], (8, 128)))
        return (x, ctx_2048, mask_BxS2_bk0)
    x, ctx_2048, mask_BxS2_bk0 = _rec_inputs()

    def _L0_xattn_setup():
        import jax, jax.numpy as jnp
        import numpy as np
        H = 256
        NH = 16
        HD = H // NH
        EPS = 1e-06

        def rmsnorm(x, w, eps=EPS):
            var = jnp.mean(x * x, axis=-1, keepdims=True)
            return x * jax.lax.rsqrt(var + eps) * w
        key = jax.random.key(seed)
        ks = jax.random.split(key, 9)
        B, L, M = (4, 512, 32)
        s = 1.0 / np.sqrt(H)
        return {'hidden_states': jax.random.normal(ks[0], (B, L, H), dtype=jnp.float32), 'memory_tokens': jax.random.normal(ks[1], (B, M, H), dtype=jnp.float32), 'memory_mask': jax.random.randint(ks[2], (B, M), 0, 2).astype(bool), 'norm_w': jnp.ones((H,), dtype=jnp.float32), 'wq': jax.random.normal(ks[3], (H, H), dtype=jnp.float32) * s, 'wk': jax.random.normal(ks[4], (H, H), dtype=jnp.float32) * s, 'wv': jax.random.normal(ks[5], (H, H), dtype=jnp.float32) * s, 'wo': jax.random.normal(ks[6], (H, H), dtype=jnp.float32) * s, 'wg': jax.random.normal(ks[7], (H, H), dtype=jnp.float32) * s}
    _L0_xattn_all = _L0_xattn_setup()
    _L0_xattn_in = {k: v for k, v in _L0_xattn_all.items() if k in ('norm_w', 'wq', 'wk', 'wv', 'wo', 'wg')}
    del _L0_xattn_all

    def _L0_ffn_setup():
        import jax, jax.numpy as jnp
        import numpy as np
        GROUP_SIZE = 64

        def ternary_quant(w_fp32, g=GROUP_SIZE):
            w = w_fp32.astype(jnp.bfloat16)
            w_g = w.reshape(-1, g)
            scale = jnp.clip(jnp.mean(jnp.abs(w_g), axis=-1, keepdims=True), 1e-08, None)
            q = jnp.clip(jnp.round(w_g / scale), -1, 1)
            w_hat = (q * scale).reshape(w.shape)
            return w + jax.lax.stop_gradient(w_hat - w)

        def rms_norm(x):
            eps = jnp.finfo(x.dtype).eps.astype(jnp.float32)
            xf = x.astype(jnp.float32)
            inv = jax.lax.rsqrt(jnp.mean(xf * xf, axis=-1, keepdims=True) + eps)
            return (xf * inv).astype(x.dtype)
        key = jax.random.key(seed)
        k1, k2, k3 = jax.random.split(key, 3)
        B, S, D = (2, 256, 256)
        H = 4 * D
        x = jax.random.normal(k1, (B, S, D), dtype=jnp.float32).astype(jnp.bfloat16)
        w_gate_up = jax.random.normal(k2, (2 * H, D), dtype=jnp.float32) * 0.02
        w_proj = jax.random.normal(k3, (D, H), dtype=jnp.float32) * 0.02
        return {'x': x, 'w_gate_up': w_gate_up, 'w_proj': w_proj}
    _L0_ffn_all = _L0_ffn_setup()
    _L0_ffn_in = {k: v for k, v in _L0_ffn_all.items() if k in ('w_gate_up', 'w_proj')}
    del _L0_ffn_all

    def _L1_xattn_setup():
        import jax, jax.numpy as jnp
        import numpy as np
        B, S, DIM, HD = (4, 128, 256, 128)
        H = DIM // HD
        GN_EPS = 0.001

        def _decay_masks(n_heads, seq_len):
            gam = 1.0 - 2.0 ** (-5.0 - jnp.arange(n_heads, dtype=jnp.float32))
            idx = jnp.arange(seq_len, dtype=jnp.float32)
            expo = idx[None, :] - idx[:, None]
            D = jnp.where(expo[None, :, :] <= 0, gam[:, None, None] ** expo[None, :, :], 0.0)
            return D / jnp.sqrt(D.sum(axis=-1))[:, None, :]
        key = jax.random.key(seed)
        ks = jax.random.split(key, 8)
        x = jax.random.normal(ks[0], (B, S, DIM), dtype=jnp.float32)
        k = jax.random.normal(ks[1], (B, S, DIM), dtype=jnp.float32)
        v = jax.random.normal(ks[2], (B, S, DIM), dtype=jnp.float32)
        Wh = jax.random.normal(ks[3], (H, HD, HD), dtype=jnp.float32) / np.sqrt(HD)
        wg_w = jax.random.normal(ks[4], (DIM, DIM), dtype=jnp.float32) / np.sqrt(DIM)
        wo_w = jax.random.normal(ks[5], (DIM, DIM), dtype=jnp.float32) / np.sqrt(DIM)
        gn_gamma = jnp.ones((DIM,), dtype=jnp.float32)
        gn_beta = jnp.zeros((DIM,), dtype=jnp.float32)
        return {'x': x, 'k': k, 'v': v, 'Wh': Wh, 'wg_w': wg_w, 'wo_w': wo_w, 'gn_gamma': gn_gamma, 'gn_beta': gn_beta}
    _L1_xattn_all = _L1_xattn_setup()
    _L1_xattn_in = {k: v for k, v in _L1_xattn_all.items() if k in ('Wh', 'wg_w', 'wo_w', 'gn_gamma', 'gn_beta')}
    del _L1_xattn_all

    def _L1_ffn_setup():
        import jax, jax.numpy as jnp
        import numpy as np
        BLOCK_SIZE = 32
        HIDDEN_SIZE = 256
        MLP_DIM = 2048
        NVFP4_LUT = jnp.array([0.0, 0.5, 1.0, 1.5, 2.0, 3.0, 4.0, 6.0, 0.0, -0.5, -1.0, -1.5, -2.0, -3.0, -4.0, -6.0], dtype=jnp.float32)

        def dequant_nvfp4(W_packed, scales, block=BLOCK_SIZE):
            N = W_packed.shape[0]
            low = W_packed & 15
            high = W_packed >> 4 & 15
            idx = jnp.stack([low, high], axis=-1).reshape(N, -1)
            vals = NVFP4_LUT[idx]
            K = vals.shape[1]
            vals = vals.reshape(N, K // block, block) * scales[:, :, None]
            return vals.reshape(N, K)
        key = jax.random.key(seed)
        ks = jax.random.split(key, 7)
        x = jax.random.normal(ks[0], (4, 32, HIDDEN_SIZE), dtype=jnp.float32)
        gate_W_packed = jax.random.randint(ks[1], (MLP_DIM, HIDDEN_SIZE // 2), 0, 32, dtype=jnp.int32)
        gate_scales = jax.random.uniform(ks[2], (MLP_DIM, HIDDEN_SIZE // BLOCK_SIZE), dtype=jnp.float32) * 0.1 + 0.001
        up_W_packed = jax.random.randint(ks[3], (MLP_DIM, HIDDEN_SIZE // 2), 0, 32, dtype=jnp.int32)
        up_scales = jax.random.uniform(ks[4], (MLP_DIM, HIDDEN_SIZE // BLOCK_SIZE), dtype=jnp.float32) * 0.1 + 0.001
        down_W_packed = jax.random.randint(ks[5], (HIDDEN_SIZE, MLP_DIM // 2), 0, 32, dtype=jnp.int32)
        down_scales = jax.random.uniform(ks[6], (HIDDEN_SIZE, MLP_DIM // BLOCK_SIZE), dtype=jnp.float32) * 0.1 + 0.001
        return {'x': x, 'gate_W_packed': gate_W_packed, 'gate_scales': gate_scales, 'up_W_packed': up_W_packed, 'up_scales': up_scales, 'down_W_packed': down_W_packed, 'down_scales': down_scales}
    _L1_ffn_all = _L1_ffn_setup()
    _L1_ffn_in = {k: v for k, v in _L1_ffn_all.items() if k in ('gate_W_packed', 'gate_scales', 'up_W_packed', 'up_scales', 'down_W_packed', 'down_scales')}
    del _L1_ffn_all
    return {'x': x, 'ctx_2048': ctx_2048, 'mask_BxS2_bk0': mask_BxS2_bk0, 'L0_xattn_norm_w': _L0_xattn_in['norm_w'], 'L0_xattn_wq': _L0_xattn_in['wq'], 'L0_xattn_wk': _L0_xattn_in['wk'], 'L0_xattn_wv': _L0_xattn_in['wv'], 'L0_xattn_wo': _L0_xattn_in['wo'], 'L0_xattn_wg': _L0_xattn_in['wg'], 'L0_ffn_w_gate_up': _L0_ffn_in['w_gate_up'], 'L0_ffn_w_proj': _L0_ffn_in['w_proj'], 'L1_xattn_Wh': _L1_xattn_in['Wh'], 'L1_xattn_wg_w': _L1_xattn_in['wg_w'], 'L1_xattn_wo_w': _L1_xattn_in['wo_w'], 'L1_xattn_gn_gamma': _L1_xattn_in['gn_gamma'], 'L1_xattn_gn_beta': _L1_xattn_in['gn_beta'], 'L1_ffn_gate_W_packed': _L1_ffn_in['gate_W_packed'], 'L1_ffn_gate_scales': _L1_ffn_in['gate_scales'], 'L1_ffn_up_W_packed': _L1_ffn_in['up_W_packed'], 'L1_ffn_up_scales': _L1_ffn_in['up_scales'], 'L1_ffn_down_W_packed': _L1_ffn_in['down_W_packed'], 'L1_ffn_down_scales': _L1_ffn_in['down_scales']}

def reference(x, ctx_2048, mask_BxS2_bk0, L0_xattn_norm_w, L0_xattn_wq, L0_xattn_wk, L0_xattn_wv, L0_xattn_wo, L0_xattn_wg, L0_ffn_w_gate_up, L0_ffn_w_proj, L1_xattn_Wh, L1_xattn_wg_w, L1_xattn_wo_w, L1_xattn_gn_gamma, L1_xattn_gn_beta, L1_ffn_gate_W_packed, L1_ffn_gate_scales, L1_ffn_up_W_packed, L1_ffn_up_scales, L1_ffn_down_W_packed, L1_ffn_down_scales):
    import jax
    import jax.numpy as jnp

    def _L0_xattn_ref(hidden_states, memory_tokens, memory_mask, norm_w, wq, wk, wv, wo, wg):
        import jax, jax.numpy as jnp
        import numpy as np
        H = 256
        NH = 16
        HD = H // NH
        EPS = 1e-06

        def rmsnorm(x, w, eps=EPS):
            var = jnp.mean(x * x, axis=-1, keepdims=True)
            return x * jax.lax.rsqrt(var + eps) * w
        B, L, C = hidden_states.shape
        M = memory_tokens.shape[1]
        scale = HD ** (-0.5)
        x = rmsnorm(hidden_states, norm_w)
        q = (x @ wq.T).reshape(B, L, NH, HD)
        k = (memory_tokens @ wk.T).reshape(B, M, NH, HD)
        v = (memory_tokens @ wv.T).reshape(B, M, NH, HD)
        attn = jnp.einsum('blhd,bmhd->bhlm', q, k) * scale
        attn = jnp.where(memory_mask[:, None, None, :], attn, -jnp.inf)
        attn = jax.nn.softmax(attn, axis=-1)
        attn = jnp.nan_to_num(attn, nan=0.0)
        out = jnp.einsum('bhlm,bmhd->blhd', attn, v).reshape(B, L, C)
        out = out @ wo.T
        gate = jax.nn.sigmoid(x @ wg.T)
        return gate * out

    def _L0_ffn_ref(x, w_gate_up, w_proj):
        import jax, jax.numpy as jnp
        import numpy as np
        GROUP_SIZE = 64

        def ternary_quant(w_fp32, g=GROUP_SIZE):
            w = w_fp32.astype(jnp.bfloat16)
            w_g = w.reshape(-1, g)
            scale = jnp.clip(jnp.mean(jnp.abs(w_g), axis=-1, keepdims=True), 1e-08, None)
            q = jnp.clip(jnp.round(w_g / scale), -1, 1)
            w_hat = (q * scale).reshape(w.shape)
            return w + jax.lax.stop_gradient(w_hat - w)

        def rms_norm(x):
            eps = jnp.finfo(x.dtype).eps.astype(jnp.float32)
            xf = x.astype(jnp.float32)
            inv = jax.lax.rsqrt(jnp.mean(xf * xf, axis=-1, keepdims=True) + eps)
            return (xf * inv).astype(x.dtype)
        wq_gu = ternary_quant(w_gate_up)
        gu = jnp.einsum('bsd,hd->bsh', x, wq_gu)
        gate, up = jnp.split(gu, 2, axis=-1)
        h = jax.nn.silu(gate) * up
        hn = rms_norm(h)
        wq_p = ternary_quant(w_proj)
        return jnp.einsum('bsh,dh->bsd', hn, wq_p)

    def _L1_xattn_ref(x, k, v, Wh, wg_w, wo_w, gn_gamma, gn_beta):
        import jax, jax.numpy as jnp
        import numpy as np
        B, S, DIM, HD = (4, 128, 256, 128)
        H = DIM // HD
        GN_EPS = 0.001

        def _decay_masks(n_heads, seq_len):
            gam = 1.0 - 2.0 ** (-5.0 - jnp.arange(n_heads, dtype=jnp.float32))
            idx = jnp.arange(seq_len, dtype=jnp.float32)
            expo = idx[None, :] - idx[:, None]
            D = jnp.where(expo[None, :, :] <= 0, gam[:, None, None] ** expo[None, :, :], 0.0)
            return D / jnp.sqrt(D.sum(axis=-1))[:, None, :]
        b, s, dim = x.shape
        h, hd, _ = Wh.shape
        xh = x.reshape(b, s, h, hd)
        kh = k.reshape(b, s, h, hd)
        vh = v.reshape(b, s, h, hd)
        Q = jnp.einsum('bshd,hde->bshe', xh, Wh)
        K = jnp.einsum('bshd,hde->bshe', kh, Wh)
        V = jnp.einsum('bshd,hde->bshe', vh, Wh)
        scores = jnp.einsum('bshe,bthe->bhst', Q, K) / jnp.sqrt(jnp.float32(hd))
        Dn = _decay_masks(h, s)
        masked = scores * Dn[None, :, :, :]
        A = jnp.maximum(jnp.abs(masked.sum(axis=0)), 1.0)
        O = jnp.einsum('hst,bthe->bshe', A, V).reshape(b, s, dim)
        mu = O.mean(axis=-1, keepdims=True)
        var = O.var(axis=-1, keepdims=True)
        Y = (O - mu) / jnp.sqrt(var + GN_EPS) * gn_gamma + gn_beta
        W = jax.nn.relu(x @ wg_w)
        return W * Y @ wo_w

    def _L1_ffn_ref(x, gate_W_packed, gate_scales, up_W_packed, up_scales, down_W_packed, down_scales):
        import jax, jax.numpy as jnp
        import numpy as np
        BLOCK_SIZE = 32
        HIDDEN_SIZE = 256
        MLP_DIM = 2048
        NVFP4_LUT = jnp.array([0.0, 0.5, 1.0, 1.5, 2.0, 3.0, 4.0, 6.0, 0.0, -0.5, -1.0, -1.5, -2.0, -3.0, -4.0, -6.0], dtype=jnp.float32)

        def dequant_nvfp4(W_packed, scales, block=BLOCK_SIZE):
            N = W_packed.shape[0]
            low = W_packed & 15
            high = W_packed >> 4 & 15
            idx = jnp.stack([low, high], axis=-1).reshape(N, -1)
            vals = NVFP4_LUT[idx]
            K = vals.shape[1]
            vals = vals.reshape(N, K // block, block) * scales[:, :, None]
            return vals.reshape(N, K)
        B, S, H = x.shape
        xt = x.reshape(B * S, H)
        Wg = dequant_nvfp4(gate_W_packed, gate_scales)
        Wu = dequant_nvfp4(up_W_packed, up_scales)
        Wd = dequant_nvfp4(down_W_packed, down_scales)
        gate = jnp.einsum('th,nh->tn', xt, Wg)
        up = jnp.einsum('th,nh->tn', xt, Wu)
        gelu = jnp.tanh(0.7978845608028654 * (gate + 0.044715 * gate ** 3)) * gate * 0.5 + gate * 0.5
        inter = gelu * up
        out = jnp.einsum('tn,hn->th', inter, Wd)
        return out.reshape(B, S, H)
    x = x + _L0_xattn_ref(_layernorm(x, axis=-1), ctx_2048, mask_BxS2_bk0, L0_xattn_norm_w, L0_xattn_wq, L0_xattn_wk, L0_xattn_wv, L0_xattn_wo, L0_xattn_wg)
    x = x + _L0_ffn_ref(_layernorm(x, axis=-1), L0_ffn_w_gate_up, L0_ffn_w_proj)
    x = x + _L1_xattn_ref(_layernorm(x, axis=-1), ctx_2048, ctx_2048, L1_xattn_Wh, L1_xattn_wg_w, L1_xattn_wo_w, L1_xattn_gn_gamma, L1_xattn_gn_beta)
    x = x + _L1_ffn_ref(_layernorm(x, axis=-1), L1_ffn_gate_W_packed, L1_ffn_gate_scales, L1_ffn_up_W_packed, L1_ffn_up_scales, L1_ffn_down_W_packed, L1_ffn_down_scales)
    return x

_drawn_inputs = setup_inputs


def setup_inputs(seed=0):
    import zlib

    import numpy as np

    out = dict(_drawn_inputs(seed))
    spreads = {'L0_xattn_norm_w': (1.0, 0.2),
     'L1_xattn_gn_gamma': (1.0, 0.2),
     'L1_xattn_gn_beta': (0.0, 0.1)}
    factors = {}
    for name, (base, spread) in spreads.items():
        noise = np.random.default_rng([zlib.crc32(name.encode()), seed]).standard_normal(out[name].shape)
        drawn = base * np.exp(spread * noise) if base else spread * noise
        out[name] = jnp.asarray(drawn.astype(out[name].dtype))
    for name, factor in factors.items():
        out[name] = (out[name] * factor).astype(out[name].dtype)
    return out
```

```python
from contextlib import ExitStack

import numpy as np

import concourse.bass as bass
from concourse import mybir

ALU = mybir.AluOpType
ACT = mybir.ActivationFunctionType
AX_X = mybir.AxisListType.X
F32 = mybir.dt.float32
F32R = mybir.dt.float32r
BF16 = mybir.dt.bfloat16
F16 = mybir.dt.float16
I32 = mybir.dt.int32
U8 = mybir.dt.uint8

P = 128
B = 8
D = 256
KT = D // P
TOK = B * P
CH = 512
NC = TOK // CH
BPC = CH // P
NH = 16
HD = D // NH
HPT = P // HD
HC = 32
HB = P // HC
HID0 = 1024
HT0 = HID0 // P
HID1 = 2048
JT1 = HID1 // (2 * P)
WCOL = 768
TP = HT0 * WCOL // CH
H1 = 2
SCALE = float(HD) ** -0.5
BIG = 1.0e30
TINY = 1.0e-30
EPS_LN = 1e-5
EPS_RMS = 1e-6
EPS_GN = 1e-3
EPS_F32 = float(np.finfo(np.float32).eps)
V1_ORDER = (2, 3, 0, 1)
W_K, W_V, W_Q, W_G, W_O = range(5)
C_DECAY, C_IDENT, C_HEAD, C_GROUP, C_END = 0, 256, 384, 392, 520


def build(nc, t):
    ctx = ExitStack()
    with ctx:
        def sem(name):
            return ctx.enter_context(nc.semaphore(name))

        def sb(name, shape, dt=F32, scope=ctx):
            return scope.enter_context(nc.sbuf_tensor(name, shape, dt))

        ps = ctx.enter_context(nc.psum_tensor("ps", [P, 8, CH], F32))
        bank = [ps[:, i, :] for i in range(8)]

        cst = sb("cst", [P, C_END])
        x = sb("x", [P, B, D])
        xn = sb("xn", [P, B, D])
        xth = sb("xth", [P, KT, TOK], F32R)
        xtl = sb("xtl", [P, KT, TOK], F32R)
        gate = sb("gate", [P, B, D])
        ct = sb("ct", [P, KT, TOK])
        w1 = sb("w1", [P, 2 * KT * D + H1 * P])
        w1h = sb("w1h", [P, 2 * KT * D + H1 * P], F32R)
        w1l = sb("w1l", [P, 2 * KT * D + H1 * P], F32R)
        tern = sb("tern", [P, HT0 + 1, WCOL], BF16)
        normw = sb("normw", [P, KT])
        gamma = sb("gamma", [P, D])
        beta = sb("beta", [P, D])
        stats = sb("stats", [P, B, 6])
        mv = sb("mv", [P, B, 2])
        va = sb("va", [P, B])
        rs = sb("rs", [P, B])
        mhalf = sb("mhalf", [P, B])
        onesf = sb("onesf", [P, 1])
        unread = sb("unread", [P, 16])
        zero_r = sb("zero_r", [P, P], F32R)
        groupb = sb("groupb", [P, P], BF16)
        ident = cst[:, C_IDENT:C_IDENT + P]
        headm = cst[:, C_HEAD:C_HEAD + HPT]

        s1 = ExitStack()
        w0h = sb("w0h", [P, 5, KT, D], F32R, s1)
        w0l = sb("w0l", [P, 5, KT, D], F32R, s1)
        kh = sb("kh", [P, KT, TOK], F32R, s1)
        kl = sb("kl", [P, KT, TOK], F32R, s1)
        vp = sb("vp", [P, B, NH * (HD + 1) + HC - HD - 1], F32, s1)
        pt = sb("pt", [P, 2, HPT, P], F32, s1)
        maskc8 = sb("maskc8", [P, B // 4], I32, s1)
        maskc = sb("maskc", [P, B], F32, s1)
        maskb = sb("maskb", [P, B], F32, s1)
        maskr8 = sb("maskr8", [1, TOK // 4], I32, s1)
        maskr = sb("maskr", [P, TOK], F32R, s1)
        ones_r = sb("ones_r", [P, P], F32R, s1)
        mx = sb("mx", [P, 2, HPT], F32, s1)
        mdiag = sb("mdiag", [P, 2, HPT, P], F32R, s1)
        avt = sb("avt", [P, CH], F32, s1)
        den = sb("den", [P, NH], F32, s1)
        rden = sb("rden", [P, NH], F32, s1)
        traw = sb("traw", [P, 2, CH], F32, s1)
        tab = sb("tab", [P, 3, CH], BF16, s1)
        tsg = sb("tsg", [P, 3, CH], BF16, s1)
        tsc = sb("tsc", [P, CH], BF16, s1)
        tgt = sb("tgt", [P, CH], BF16, s1)
        tdf = sb("tdf", [P, CH], BF16, s1)
        trd = sb("trd", [P, CH], BF16, s1)
        tmg = sb("tmg", [P, 2, CH], BF16, s1)
        s1a = ExitStack()
        cth = sb("cth", [P, KT, TOK], F32R, s1a)
        ctl = sb("ctl", [P, KT, TOK], F32R, s1a)
        w0 = sb("w0", [P, 5, KT, D], F32, s1a)
        s1a.close()
        qh = sb("qh", [P, KT, TOK], F32R, s1)
        ql = sb("ql", [P, KT, TOK], F32R, s1)
        km = sb("km", [P, 2, HPT, P], F32R, s1)
        qhm = sb("qhm", [P, 2, HPT, P], F32R, s1)
        qlm = sb("qlm", [P, 2, HPT, P], F32R, s1)
        s1.close()

        s2 = ExitStack()
        k1t = sb("k1t", [P, H1, TOK], F32, s2)
        v1 = sb("v1", [P, H1, B, P], F32, s2)
        q1t = sb("q1t", [P, H1, TOK], F32, s2)
        shift = sb("shift", [P, B, D], F32, s2)
        a1 = sb("a1", [P, H1, P], F32, s2)
        a1m = sb("a1m", [P, H1, P], F32, s2)
        o1 = sb("o1", [P, B, H1, P], F32, s2)
        acc = sb("acc", [P, NC, CH], F32, s2)
        sq = sb("sq", [P, 2, CH], F32, s2)
        gact = sb("gact", [P, 2, CH], F32, s2)
        mid = sb("mid", [P, 2, CH], F32, s2)
        hidh = sb("hidh", [P, 2, CH], F32R, s2)
        hidl = sb("hidl", [P, 2, CH], F32R, s2)
        slot0 = sb("slot0", [P, 2, WCOL], F32R, s2)
        packed = sb("packed", [P, 2, WCOL], I32, s2)
        scl = sb("scl", [P, 2, WCOL], F32, s2)
        code = sb("code", [P, WCOL], I32, s2)
        mag = sb("mag", [P, WCOL], I32, s2)
        sgn = sb("sgn", [P, WCOL], I32, s2)
        wf = sb("wf", [P, 2, WCOL], F32, s2)
        slh = sb("slh", [P, 2, 2, WCOL], F32R, s2)
        sll = sb("sll", [P, 2, 2, WCOL], F32R, s2)
        s2.close()

        in_cst, in_ctx, in_wkv, in_w0, in_x, in_w1, in_small, in_mask = map(
            sem, ("in_cst", "in_ctx", "in_wkv", "in_w0", "in_x", "in_w1", "in_small", "in_mask"))
        in_tern = [sem(f"in_tern{i}") for i in range(2)]
        in_pack = [sem(f"in_pack{i}") for i in range(2)]
        out_sent = sem("out_sent")
        pool_set = sem("pool_set")
        group_ready = sem("group_ready")
        ctx_hi, ctx_lo = sem("ctx_hi"), sem("ctx_lo")
        wkv_hi, wkv_lo, w0_hi, w0_lo = sem("wkv_hi"), sem("wkv_lo"), sem("w0_hi"), sem("w0_lo")
        w1_hi, w1_lo = sem("w1_hi"), sem("w1_lo")
        masks_ready = sem("masks_ready")
        dve_chain, act_chain, pool_chain = sem("dve_chain"), sem("act_chain"), sem("pool_chain")
        k_full, k_hi, k_lo = sem("k_full"), sem("k_hi"), sem("k_lo")
        v_full, v_done = sem("v_full"), sem("v_done")
        q_full, q_hi, q_lo = sem("q_full"), sem("q_hi"), sem("q_lo")
        g_full, g_done = sem("g_full"), sem("g_done")
        km_ready, qhm_ready, qlm_ready = sem("km_ready"), sem("qhm_ready"), sem("qlm_ready")
        s_full, max_done = sem("s_full"), sem("max_done")
        md_done, a_step, t_step = sem("md_done"), sem("a_step"), sem("t_step")
        st_full, exp_done = sem("st_full"), sem("exp_done")
        av_full, av_copied, rows_full, att_done = sem("av_full"), sem("av_copied"), sem("rows_full"), sem("att_done")
        t_abs, t_sign = sem("t_abs"), sem("t_sign")
        t_mean, t_scale, t_mag, t_done = sem("t_mean"), sem("t_scale"), sem("t_mag"), sem("t_done")
        NT = 6
        var_ready = [sem(f"var_ready{i}") for i in range(NT)]
        rstd_ready = [sem(f"rstd_ready{i}") for i in range(NT)]
        xn_ready = [sem(f"xn_ready{i}") for i in range(NT)]
        xt_full = [sem(f"xt_full{i}") for i in range(NT)]
        xt_hi = [sem(f"xt_hi{i}") for i in range(NT)]
        xt_lo = [sem(f"xt_lo{i}") for i in range(NT)]
        wo_full, wo_done = sem("wo_full"), sem("wo_done")
        k1_full, k1_done, v1_full, v1_done = sem("k1_full"), sem("k1_done"), sem("v1_full"), sem("v1_done")
        q1_full, q1_done = sem("q1_full"), sem("q1_done")
        g1_full, g1_done, gated = sem("g1_full"), sem("g1_done"), sem("gated")
        g_step = sem("g_step")
        s1_full, a1_ready = sem("s1_full"), sem("a1_ready")
        o1_full, o1_done = sem("o1_full"), sem("o1_done")
        wo1_full, wo1_done = sem("wo1_full"), sem("wo1_done")
        fs = [{n: sem(f"f{l}_{n}") for n in (
            "slot_ready", "gate_full", "up_full", "act_done", "pair_free", "hi_done",
            "hid_ready", "down_turn", "sq_done", "acc_done", "down_full", "down_done",
            "code", "mag", "or", "wf_ready", "w_hi")} for l in range(2)]
        ms_full, ms_scaled, ms_rstd = sem("ms_full"), sem("ms_scaled"), sem("ms_rstd")

        block = ctx.enter_context(nc.Block())

        def wg1(part, k):
            return part[:, k * D:(k + 1) * D]

        def wo1(part, k):
            return part[:, (KT + k) * D:(KT + k + 1) * D]

        def wh1(part, h):
            return part[:, 2 * KT * D + h * P:2 * KT * D + (h + 1) * P]

        def cols(c):
            return slice(c * CH, (c + 1) * CH)

        def toks(b):
            return slice(b * P, (b + 1) * P)

        def scope1_over(eng):
            eng.wait_ge(wo_full, B // 2)
            eng.wait_ge(att_done, B)
            eng.wait_ge(t_done, TP)

        def per_head(ap):
            return ap[:, None, :].broadcast_to([P, HPT, P])

        @block.sync
        def _(sp):
            sp.dma_start(w0[:, 0:W_Q, :, :], t["w0"][:, 0:W_Q]).then_inc(in_wkv, 16)
            for c in range(NC):
                if c:
                    sp.wait_ge(in_ctx, 16 * c)
                sp.dma_start(ct[:, :, cols(c)], t["ctx"][:, :, cols(c)]).then_inc(in_ctx, 16)
            sp.dma_start(cst[:, :], t["cst"]).then_inc(in_cst, 16)
            sp.dma_start(w0[:, W_Q:, :, :], t["w0"][:, W_Q:]).then_inc(in_w0, 16)
            sp.dma_start(w1[:, :], t["w1"]).then_inc(in_w1, 16)
            for i in range(TP):
                if i >= 2:
                    sp.wait_ge(t_sign, i - 1)
                sp.dma_start(traw[:, i % 2, :], t["tern"][:, i * CH:(i + 1) * CH]).then_inc(in_tern[i % 2], 16)
            scope1_over(sp)

            def load_pair(slot, src):
                sp.dma_start(packed[:, slot:slot + 1, :], t["packed"][:, src, :]).then_inc(in_pack[slot], 16)
                sp.dma_start(scl[:, slot, :], t["scl"](src)).then_inc(in_pack[slot], 16)

            load_pair(0, bass.ds(0, 1))
            load_pair(1, bass.ds(1, 1))
            with sp.Fori(0, JT1 // 2 - 1) as i:
                for s in range(2):
                    sp.wait_ge(fs[1]["wf_ready"], i * 4 + 2 * s + 2)
                    load_pair(s, bass.ds(i * 2 + s + 2, 1))
            sp.wait_ge(fs[1]["wf_ready"], 2 * (JT1 - 1))
            load_pair(0, bass.ds(JT1 - 1, 1))
            for r in range(B // 2):
                sp.wait_ge(fs[1]["down_done"], r + 1)
                sp.dma_start(t["out"][:, 2 * r:2 * r + 2, :], x[:, 2 * r:2 * r + 2, :]).then_inc(out_sent, 16)
            sp.wait_ge(out_sent, 16 * (B // 2))

        @block.gpsimd
        def _(pool):
            n = [0]

            def link(ins):
                n[0] += 1
                ins.then_inc(pool_chain, 1)
                pool.wait_ge(pool_chain, n[0])

            pool.memset(zero_r[:, :].bitcast(F32), 0.0)
            pool.memset(mhalf[:, :], -0.5)
            pool.memset(onesf[:, :], 1.0)
            pool.memset(tern[:, HT0, :], 0.0)
            pool.memset(vp[:, :, NH * (HD + 1):], 0.0)
            pool.memset(maskr[:, :].bitcast(F32), 0.0)
            pool.memset(ones_r[:, :].bitcast(F32), 1.0).then_inc(pool_set, 1)

            def rstd(i, chunks=range(NC)):
                for c in chunks:
                    s = slice(c * BPC, (c + 1) * BPC)
                    pool.wait_ge(var_ready[i], c + 1)
                    pool.tensor_tensor(rs[:, s], va[:, s], mhalf[:, s], ALU.pow).then_inc(rstd_ready[i], 1)

            rstd(0)
            pool.wait_ge(w0_hi, 1)
            pool.tensor_tensor(w0l[:, W_Q:, :, :], w0[:, W_Q:, :, :], w0h[:, W_Q:, :, :].bitcast(F32),
                               ALU.subtract).then_inc(w0_lo, 1)
            pool.wait_ge(w1_hi, 1)
            pool.tensor_tensor(w1l[:, :], w1[:, :], w1h[:, :].bitcast(F32), ALU.subtract).then_inc(w1_lo, 1)

            def masked_keys(u):
                b, hd = divmod(u, KT)
                if u >= 2:
                    pool.wait_ge(s_full, u - 1)
                pool.tensor_tensor(km[:, u % 2, :, :], per_head(kh[:, hd, toks(b)].bitcast(F32)),
                                   headm[:, :, None].broadcast_to([P, HPT, P]), ALU.mult).then_inc(km_ready, 1)

            def masked_queries(u):
                b, hd = divmod(u, KT)
                if u == 0:
                    pool.wait_ge(q_hi, NC * KT)
                if u >= 2:
                    pool.wait_ge(st_full, u - 1)
                pool.tensor_tensor(qhm[:, u % 2, :, :], per_head(qh[:, hd, toks(b)].bitcast(F32)),
                                   headm[:, :, None].broadcast_to([P, HPT, P]), ALU.mult).then_inc(qhm_ready, 1)

            def signed_weights(i):
                pool.wait_ge(t_mag, i + 1)
                pool.wait_ge(t_sign, i + 1)
                pool.tensor_tensor(tern[:, 0:HT0, :].rearrange("p t w -> p (t w)")[:, i * CH:(i + 1) * CH],
                                   tmg[:, i % 2, :], tsg[:, i % 3, :], ALU.mult).then_inc(t_done, 1)

            pool.wait_ge(k_hi, NC * KT)
            pool.wait_ge(v_full, B // 2)
            pool.wait_ge(wkv_lo, 1)
            pool.wait_ge(w0_lo, 1)
            for u in range(-3, B * KT):
                if 0 <= u - 2 < TP:
                    signed_weights(u - 2)
                if 0 <= u + 1 < B * KT:
                    masked_queries(u + 1)
                if u + 3 < B * KT:
                    masked_keys(u + 3)

            scope1_over(pool)
            pool.memset(hidh[:, 1, :].bitcast(F32), 0.0).then_inc(fs[0]["down_turn"], 1)
            pool.memset(hidl[:, 1, :].bitcast(F32), 0.0).then_inc(fs[0]["down_turn"], 1)
            pool.memset(slot0[:, 1, :].bitcast(F32), 0.0).then_inc(fs[0]["down_turn"], 1)
            pool.memset(acc[:, :, :], 0.0).then_inc(fs[0]["down_turn"], 1)
            pool.wait_ge(fs[0]["down_turn"], 4)
            pool.memset(sq[:, 0, 0:1], 0.0).then_inc(fs[0]["hid_ready"], 1)
            pool.memset(mid[:, 1, :], 0.0).then_inc(fs[0]["acc_done"], 1)
            pool.memset(unread[:, 0:1], 0.0).then_inc(fs[0]["acc_done"], 1)

            rstd(2)

            f = fs[0]

            def add_squares(k, u):
                pool.wait_ge(f["sq_done"], k + 1)
                pool.wait_ge(f["acc_done"], k + 1)
                pool.tensor_tensor(acc[:, 1 - u % 2, :], acc[:, 1 - u % 2, :], sq[:, u % 2, :],
                                   ALU.add).then_inc(f["acc_done"], 1)

            with pool.Fori(0, HT0 // 2) as i:
                for u in range(4):
                    add_squares(i * 4 + u, u)
            add_squares(2 * HT0, 0)

            for c in range(NC):
                s = slice(c * BPC, (c + 1) * BPC)
                pool.wait_ge(ms_scaled, c + 1)
                pool.tensor_tensor(rs[:, s], va[:, s], mhalf[:, s], ALU.pow).then_inc(ms_rstd, 1)
                rstd(3, [c])

            f = fs[1]
            pool.memset(slh[:, 1, :, :].bitcast(F32), 0.0).then_inc(f["down_turn"], 1)
            pool.memset(sll[:, 1, :, :].bitcast(F32), 0.0).then_inc(f["down_turn"], 1)
            pool.wait_ge(fs[0]["down_full"], B // 2)
            pool.memset(hidh[:, 1, :].bitcast(F32), 0.0).then_inc(f["down_turn"], 1)
            pool.memset(hidl[:, 1, :].bitcast(F32), 0.0).then_inc(f["down_turn"], 1)
            pool.wait_ge(f["down_turn"], 4)
            pool.memset(sq[:, 0, 0:1], 0.0).then_inc(f["hid_ready"], 1)

            def low_weights(j, slot):
                pool.wait_ge(f["w_hi"], j + 1)
                pool.tensor_tensor(sll[:, slot, :, :], wf[:, :, :], slh[:, slot, :, :].bitcast(F32),
                                   ALU.subtract).then_inc(f["slot_ready"], 1)

            for c in range(NC):
                s = slice(c * BPC, (c + 1) * BPC)
                pool.wait_ge(g1_done, (c + 1) * BPC // 2)
                pool.tensor_tensor(shift[:, s, :], gate[:, s, :], beta[:, None, :].broadcast_to([P, BPC, D]),
                                   ALU.mult).then_inc(gated, 1)
                pool.wait_ge(gated, 2 * c + 1)
                pool.tensor_tensor(gate[:, s, :], gate[:, s, :], gamma[:, None, :].broadcast_to([P, BPC, D]),
                                   ALU.mult).then_inc(gated, 1)
            rstd(4)
            low_weights(0, 0)
            rstd(5)

            with pool.Fori(0, JT1 // 2) as i:
                for s in range(2):
                    low_weights(i * 2 + s + 1, 1 - s)

        @block.scalar
        def _(act):
            def split_hi(out, src):
                return act.activation(out, src, ACT.Copy)

            def preload(function):
                act.activation(unread[:, 0:1], mhalf[:, 0:1], function).then_inc(act_chain, 1)
                act_loads[0] += 1
                act.wait_ge(act_chain, act_loads[0])

            act_loads = [0]
            act.dma_start(normw[:, :], t["normw"]).then_inc(in_small, 16)
            act.dma_start(maskc8[:, :], t["maskc"]).then_inc(in_mask, 16)
            act.dma_start(maskr8[:, :], t["maskr"]).then_inc(in_mask, 16)
            act.wait_ge(pool_set, 1)
            preload(ACT.Copy)
            act.wait_ge(in_wkv, 16)
            for c in range(NC):
                s = slice(c * BPC, (c + 1) * BPC)
                act.dma_start(x[:, s, :], t["x"][:, s, :]).then_inc(in_x, 16)
            split_hi(w0h[:, 0:W_Q, :, :], w0[:, 0:W_Q, :, :]).then_inc(wkv_hi, 1)
            for c in range(NC):
                act.wait_ge(in_ctx, 16 * (c + 1))
                split_hi(cth[:, :, cols(c)], ct[:, :, cols(c)]).then_inc(ctx_hi, 1)
            act.dma_start(gamma[:, :], t["gamma"]).then_inc(in_small, 16)
            act.dma_start(beta[:, :], t["beta"]).then_inc(in_small, 16)
            act.wait_ge(in_w0, 16)
            split_hi(w0h[:, W_Q:, :, :], w0[:, W_Q:, :, :]).then_inc(w0_hi, 1)
            act.wait_ge(in_w1, 16)
            split_hi(w1h[:, :], w1[:, :]).then_inc(w1_hi, 1)
            for j in range(KT * NC):
                c, hd = divmod(j, KT)
                act.wait_ge(k_full, j + 1)
                split_hi(kh[:, hd, cols(c)], bank[j]).then_inc(k_hi, 1)

            def xt_high(i, chunks=range(NC)):
                for c, e in ((c, e) for c in chunks for e in range(KT)):
                    j = c * KT + e
                    act.wait_ge(xt_full[i], j + 1)
                    if i == 0:
                        act.activation(xth[:, e, cols(c)], bank[j], ACT.Copy, scale=normw[:, e:e + 1]).then_inc(xt_hi[i], 1)
                    else:
                        split_hi(xth[:, e, cols(c)], bank[j]).then_inc(xt_hi[i], 1)

            act.wait_ge(in_small, 48)
            xt_high(0)
            for j in range(KT * NC):
                c, hd = divmod(j, KT)
                act.wait_ge(q_full, j + 1)
                split_hi(qh[:, hd, cols(c)], bank[4 + j]).then_inc(q_hi, 1)
            for r in range(B // 2):
                act.wait_ge(g_full, r + 1)
                act.activation(gate[:, 2 * r:2 * r + 2, :].rearrange("p b d -> p (b d)"), bank[r],
                               ACT.Sigmoid).then_inc(g_done, 1)
            act.wait_ge(q_lo, KT * NC)

            def copy_values(b):
                act.wait_ge(av_full, 2 * b + 2)
                if b >= 1:
                    act.wait_ge(rows_full, b)
                act.activation(avt[:, :], bank[7], ACT.Copy).then_inc(av_copied, 1)

            for u in range(-1, B * KT):
                if u >= 3 and u % 2 == 1:
                    copy_values((u - 3) // 2)
                if 0 <= u < TP:
                    act.wait_ge(in_tern[u % 2], 16 * (u // 2 + 1))
                    if u >= 3:
                        act.wait_ge(t_done, u - 2)
                    act.activation(tab[:, u % 3, :], traw[:, u % 2, :], ACT.Abs).then_inc(t_abs, 1)
                    act.activation(tsg[:, u % 3, :], traw[:, u % 2, :], ACT.Sign).then_inc(t_sign, 1)
                if u + 1 < B * KT:
                    b, hd = divmod(u + 1, KT)
                    if u + 1 >= 2:
                        act.wait_ge(st_full, u)
                    for h in range(HPT):
                        act.activation(qlm[:, (u + 1) % 2, h, :], ql[:, hd, toks(b)].bitcast(F32), ACT.Copy,
                                       scale=headm[:, h:h + 1]).then_inc(qlm_ready, 1)
                if u >= 0:
                    p = 2 + 2 * (u % 2)
                    act.wait_ge(st_full, u + 1)
                    if u >= 2:
                        act.wait_ge(av_full, u - 1)
                    act.activation(pt[:, u % 2, :, :].rearrange("p h q -> p (h q)"),
                                   ps[:, p:p + 2, :].rearrange("p a n -> p (a n)"), ACT.Exp,
                                   bias=maskb[:, u // 2:u // 2 + 1], scale=SCALE).then_inc(exp_done, 1)
            xt_high(1, [0])
            copy_values(B - 1)
            xt_high(1, [1])
            scope1_over(act)
            for j in range(H1 * NC):
                h, c = divmod(j, NC)
                act.wait_ge(k1_full, j + 1)
                act.activation(k1t[:, h, cols(c)], bank[j], ACT.Copy).then_inc(k1_done, 1)
            xt_high(2)

            f = fs[0]

            def slot0_copy(tile, ready):
                act.activation(slot0[:, ready, :], tile, ACT.Copy).then_inc(f["slot_ready"], 1)

            def squares(k, u):
                act.wait_ge(f["pair_free"], k + 2)
                act.wait_ge(f["acc_done"], k + 1)
                act.activation(sq[:, u % 2, :], mid[:, 1 - u % 2, :], ACT.Square).then_inc(f["sq_done"], 1)

            preload(ACT.Silu)
            act.wait_ge(f["acc_done"], 2)
            slot0_copy(tern[:, 0, :], 0)
            with act.Fori(0, HT0 // 2) as i:
                for u in range(4):
                    s, c = divmod(u, 2)
                    act.wait_ge(f["gate_full"], i * 4 + u + 1)
                    act.activation(gact[:, c, :], bank[2 * c], ACT.Silu).then_inc(f["act_done"], 1)
                    squares(i * 4 + u, u)
                    if c == 0:
                        act.wait_ge(f["down_turn"], i * 4 + 2 * s + 5)
                        slot0_copy(tern[:, bass.ds(i * 2 + s + 1, 1), :], 1 - s)
            squares(2 * HT0, 0)

            f = fs[1]

            def high_weights(j, slot):
                act.wait_ge(f["wf_ready"], j * 2 + 2)
                act.wait_ge(f["down_turn"], j * 4 + 1)
                split_hi(slh[:, slot, :, :], wf[:, :, :]).then_inc(f["w_hi"], 1)

            for turn, j in enumerate(V1_ORDER):
                h, c = divmod(j, NC)
                act.wait_ge(v1_full, turn + 1)
                act.activation(v1[:, h, BPC * c:BPC * (c + 1), :].rearrange("p b e -> p (b e)"), bank[j],
                               ACT.Copy).then_inc(v1_done, 1)
            for c in range(NC):
                xt_high(3, [c])
                for r in range(c * BPC // 2, (c + 1) * BPC // 2):
                    act.wait_ge(g1_full, r + 1)
                    act.activation(gate[:, 2 * r:2 * r + 2, :].rearrange("p b d -> p (b d)"), bank[r],
                                   ACT.Relu).then_inc(g1_done, 1)
                for h in range(H1):
                    act.wait_ge(q1_full, c * H1 + h + 1)
                    act.activation(q1t[:, h, cols(c)], bank[4 + c * H1 + h], ACT.Copy).then_inc(q1_done, 1)
            high_weights(0, 0)
            for j in range(H1 * NC):
                c, h = divmod(j, H1)
                act.wait_ge(o1_full, j + 1)
                act.activation(o1[:, BPC * c:BPC * (c + 1), h, :], bank[j].rearrange("p (b e) -> p b e", e=P),
                               ACT.Copy).then_inc(o1_done, 1)
            xt_high(4)
            xt_high(5)
            preload(ACT.Gelu_apprx_tanh)

            with act.Fori(0, JT1 // 2) as i:
                for u in range(8):
                    act.wait_ge(f["gate_full"], i * 8 + u + 1)
                    act.activation(gact[:, u % 2, :], bank[2 * (u % 2)], ACT.Gelu_apprx_tanh).then_inc(f["act_done"], 1)
                    if u % 4 == 1:
                        high_weights(i * 2 + u // 4 + 1, 1 - u // 4)

        @block.vector
        def _(dve):
            n = [0]

            def link(ins):
                n[0] += 1
                ins.then_inc(dve_chain, 1)
                dve.wait_ge(dve_chain, n[0])

            dve.wait_ge(in_mask, 32)
            dve.wait_ge(pool_set, 1)
            link(dve.tensor_copy(maskc[:, :], maskc8[:, :].bitcast(U8)))
            link(dve.tensor_scalar(maskb[:, :], maskc[:, :], 1.0, BIG, ALU.subtract, ALU.mult))
            link(dve.tensor_scalar(maskr[0:1, :], maskr8[:, :].bitcast(U8), 1.0, BIG, ALU.subtract, ALU.mult))
            dve.wait_ge(wkv_hi, 1)
            dve.tensor_tensor(w0l[:, 0:W_Q, :, :], w0[:, 0:W_Q, :, :], w0h[:, 0:W_Q, :, :].bitcast(F32),
                              ALU.subtract).then_inc(wkv_lo, 1)
            for c in range(NC):
                dve.wait_ge(ctx_hi, c + 1)
                dve.tensor_tensor(ctl[:, :, cols(c)], ct[:, :, cols(c)], cth[:, :, cols(c)].bitcast(F32),
                                  ALU.subtract).then_inc(ctx_lo, 1)
            for b in range(B):
                ones = vp[:, b, 0:NH * (HD + 1)].rearrange("p (h d) -> p h d", d=HD + 1)[:, :, HD:HD + 1]
                dve.tensor_copy(ones, maskc[:, b:b + 1, None].broadcast_to([P, NH, 1])).then_inc(masks_ready, 1)
            dve.wait_ge(in_cst, 16)
            dve.tensor_copy(groupb[:, :], cst[:, C_GROUP:C_GROUP + P]).then_inc(masks_ready, 1)

            def norm_stats(i, c, rows, eps, slope=1.0):
                s = slice(c * BPC, (c + 1) * BPC)
                for step in range(2):
                    for b in range(s.start, s.stop):
                        n[0] += 1
                        if step == 0:
                            dve.bn_stats(stats[:, b, :], rows(b)).then_inc(dve_chain, 1)
                        else:
                            dve.bn_aggr(mv[:, b, :], stats[:, b, :]).then_inc(dve_chain, 1)
                    dve.wait_ge(dve_chain, n[0])
                dve.tensor_scalar(va[:, s], mv[:, s, 1], slope, eps, ALU.mult, ALU.add).then_inc(var_ready[i], 1)

            def norm_rows(i, c, rows):
                dve.wait_ge(rstd_ready[i], c + 1)
                for b in range(c * BPC, (c + 1) * BPC):
                    dve.tensor_scalar(xn[:, b, :], rows(b), mv[:, b, 0:1], rs[:, b:b + 1],
                                      ALU.subtract, ALU.mult).then_inc(xn_ready[i], 1)

            def xt_low(i, chunks=range(NC)):
                for c, e in ((c, e) for c in chunks for e in range(KT)):
                    j = c * KT + e
                    dve.wait_ge(xt_hi[i], j + 1)
                    hi = xth[:, e, cols(c)].bitcast(F32)
                    if i == 0:
                        dve.scalar_tensor_tensor(out=xtl[:, e, cols(c)], in0=bank[j], scalar=normw[:, e:e + 1],
                                                 in1=hi, op0=ALU.mult, op1=ALU.subtract).then_inc(xt_lo[i], 1)
                    else:
                        dve.tensor_tensor(xtl[:, e, cols(c)], bank[j], hi, ALU.subtract).then_inc(xt_lo[i], 1)

            def x_rows(b):
                return x[:, b, :]

            def keys_low(j):
                c, hd = divmod(j, KT)
                dve.wait_ge(k_hi, j + 1)
                dve.tensor_tensor(kl[:, hd, cols(c)], bank[j], kh[:, hd, cols(c)].bitcast(F32),
                                  ALU.subtract).then_inc(k_lo, 1)

            def masked_values(b):
                dve.wait_ge(v_full, b // 2 + 1)
                dve.tensor_scalar(vp[:, b, 0:NH * (HD + 1)].rearrange("p (h d) -> p h d", d=HD + 1)[:, :, 0:HD],
                                  bank[4 + b // 2][:, (b % 2) * D:(b % 2 + 1) * D].rearrange("p (h d) -> p h d", d=HD),
                                  maskc[:, b:b + 1], None, ALU.mult).then_inc(v_done, 1)

            dve.wait_ge(in_x, 32)
            for c in range(NC):
                norm_stats(0, c, x_rows, EPS_RMS * EPS_LN, 1.0 + EPS_RMS)
            for j in range(KT * NC):
                keys_low(j)
            norm_rows(0, 0, x_rows)
            for b in range(B // 2):
                masked_values(b)
            norm_rows(0, 1, x_rows)
            dve.wait_ge(in_small, 48)
            xt_low(0, [0])
            for b in range(B // 2, B):
                masked_values(b)
            xt_low(0, [1])
            for j in range(KT * NC):
                c, hd = divmod(j, KT)
                dve.wait_ge(q_hi, j + 1)
                dve.tensor_tensor(ql[:, hd, cols(c)], bank[4 + j], qh[:, hd, cols(c)].bitcast(F32),
                                  ALU.subtract).then_inc(q_lo, 1)

            def row_max(u):
                dve.wait_ge(s_full, u + 1)
                dve.tensor_reduce(mx[:, u % 2, :], ps[:, 0:2, :].rearrange("p a (h k) -> p (a h) k", k=P), AX_X,
                                  ALU.max).then_inc(max_done, 1)

            def max_diagonal(u):
                if u >= 2:
                    dve.wait_ge(st_full, u - 1)
                dve.wait_ge(max_done, u + 1)
                dve.scalar_tensor_tensor(out=mdiag[:, u % 2, :, :], in0=per_head(ident), scalar=-1.0,
                                         in1=mx[:, u % 2, :][:, :, None].broadcast_to([P, HPT, P]),
                                         op0=ALU.mult, op1=ALU.mult).then_inc(md_done, 1)

            def attention_rows(b, step):
                av = bank[7].rearrange("p (h d) -> p h d", d=HC)
                if step == 0:
                    dve.wait_ge(rows_full, b + 1)
                    dve.tensor_scalar(den[:, :], av[:, :, HD], TINY, None, ALU.max).then_inc(a_step, 1)
                elif step == 1:
                    dve.wait_ge(a_step, 2 * b + 1)
                    dve.reciprocal(rden[:, :], den[:, :]).then_inc(a_step, 1)
                else:
                    dve.wait_ge(a_step, 2 * b + 2)
                    dve.tensor_tensor(xn[:, b, :].rearrange("p (h d) -> p h d", d=HD), av[:, :, 0:HD],
                                      rden[:, :, None].broadcast_to([P, NH, HD]), ALU.mult).then_inc(att_done, 1)

            def ternary_weights(i, step):
                mag = tab[:, i % 3, :]
                if step == 0:
                    dve.wait_ge(t_mean, i + 1)
                    dve.tensor_scalar(tsc[:, :], bank[6], 1e-8, None, ALU.max).then_inc(t_scale, 1)
                elif step == 1:
                    dve.wait_ge(t_scale, i + 1)
                    dve.tensor_tensor(tdf[:, :], tsc[:, :], mag, ALU.subtract).then_inc(t_step, 1)
                elif step == 2:
                    dve.wait_ge(t_step, 3 * i + 1)
                    dve.tensor_tensor(tgt[:, :], tdf[:, :], mag, ALU.is_lt).then_inc(t_step, 1)
                elif step == 3:
                    dve.tensor_tensor(trd[:, :], mag, tdf[:, :], ALU.add).then_inc(t_step, 1)
                else:
                    dve.wait_ge(t_step, 3 * i + 3)
                    if i >= 2:
                        dve.wait_ge(t_done, i - 1)
                    dve.tensor_tensor(tmg[:, i % 2, :], trd[:, :], tgt[:, :], ALU.mult).then_inc(t_mag, 1)

            for u in range(-2, B * KT):
                tern_now, rows_now = 0 <= u - 1 < TP, u >= 3 and u % 2 == 1
                if tern_now:
                    ternary_weights(u - 1, 0)
                if 0 <= u + 1 < B * KT:
                    max_diagonal(u + 1)
                if tern_now:
                    ternary_weights(u - 1, 1)
                if u + 2 < B * KT:
                    row_max(u + 2)
                if tern_now:
                    ternary_weights(u - 1, 2)
                if rows_now:
                    attention_rows((u - 3) // 2, 0)
                if tern_now:
                    ternary_weights(u - 1, 3)
                if rows_now:
                    attention_rows((u - 3) // 2, 1)
                if tern_now:
                    ternary_weights(u - 1, 4)
                if rows_now:
                    attention_rows((u - 3) // 2, 2)
            xt_low(1, [0])
            for step in range(3):
                attention_rows(B - 1, step)
            xt_low(1, [1])

            def pair(tile, r):
                return tile[:, 2 * r:2 * r + 2, :].rearrange("p b d -> p (b d)")

            def residual(r, src):
                return dve.tensor_tensor(pair(x, r), src, pair(x, r), ALU.add)

            def chunk_pairs(c):
                return range(c * BPC // 2, (c + 1) * BPC // 2)

            for c in range(NC):
                for r in chunk_pairs(c):
                    dve.wait_ge(wo_full, r + 1)
                    dve.tensor_tensor(pair(gate, r), bank[4 + r], pair(gate, r), ALU.mult).then_inc(wo_done, 1)
                for r in chunk_pairs(c):
                    dve.wait_ge(wo_done, r + 1)
                    n[0] += 1
                    residual(r, pair(gate, r)).then_inc(dve_chain, 1)
                dve.wait_ge(dve_chain, n[0])
                if c:
                    norm_rows(2, c - 1, x_rows)
                norm_stats(2, c, x_rows, EPS_LN)
            xt_low(2, [0])
            norm_rows(2, 1, x_rows)
            xt_low(2, [1])

            f = fs[0]
            for k in range(2):
                dve.memset(unread[:, 2 + k:3 + k], 0.0).then_inc(f["pair_free"], 1)

            def hidden_rows(f, k, u):
                dve.wait_ge(f["up_full"], k + 1)
                dve.wait_ge(f["act_done"], k + 1)
                dve.tensor_tensor(mid[:, u % 2, :], bank[2 * (u % 2) + 1], gact[:, u % 2, :],
                                  ALU.mult).then_inc(f["pair_free"], 1)
                dve.wait_ge(f["pair_free"], k + 3)
                dve.wait_ge(f["down_turn"], k + 4)
                dve.tensor_copy(hidh[:, u % 2, :], mid[:, u % 2, :]).then_inc(f["hi_done"], 1)
                dve.wait_ge(f["hi_done"], k + 1)
                dve.tensor_tensor(hidl[:, u % 2, :], mid[:, u % 2, :], hidh[:, u % 2, :].bitcast(F32),
                                  ALU.subtract).then_inc(f["hid_ready"], 1)

            with dve.Fori(0, HT0 // 2) as i:
                for u in range(4):
                    dve.wait_ge(f["sq_done"], i * 4 + u + 1 if u == 0 else i * 4 + u)
                    hidden_rows(f, i * 4 + u, u)

            def mean_squares(c):
                s = slice(c * BPC, (c + 1) * BPC)
                dve.wait_ge(ms_full, c + 1)
                dve.tensor_scalar(va[:, s], bank[c][:, 0:BPC], 1.0 / HID0, EPS_F32,
                                  ALU.mult, ALU.add).then_inc(ms_scaled, 1)

            for c in range(NC):
                mean_squares(c)
                dve.wait_ge(ms_rstd, c + 1)
                for b in range(c * BPC, (c + 1) * BPC):
                    dve.wait_ge(f["down_full"], b // 2 + 1)
                    dve.scalar_tensor_tensor(out=x[:, b, :], in0=bank[4 + b // 2][:, (b % 2) * D:(b % 2 + 1) * D],
                                             scalar=rs[:, b:b + 1], in1=x[:, b, :], op0=ALU.mult,
                                             op1=ALU.add).then_inc(f["down_done"], 1)
                if c:
                    norm_rows(3, c - 1, x_rows)
                dve.wait_ge(f["down_done"], (c + 1) * BPC)
                norm_stats(3, c, x_rows, EPS_LN)
            xt_low(3, [0])
            norm_rows(3, 1, x_rows)
            xt_low(3, [1])

            f = fs[1]

            def codes(j, slot, ready):
                dve.wait_ge(in_pack[slot], ready)
                src = packed[:, slot, :]
                dve.scalar_tensor_tensor(out=code[:, :], in0=src, scalar=12, in1=src, op0=ALU.logical_shift_left,
                                         op1=ALU.bitwise_or).then_inc(f["code"], 1)
                dve.wait_ge(f["code"], j + 1)
                dve.wait_ge(f["wf_ready"], j * 2)
                dve.tensor_scalar(mag[:, :], code[:, :], 0x00070007, 9, ALU.bitwise_and,
                                  ALU.logical_shift_left).then_inc(f["mag"], 1)
                dve.tensor_scalar(sgn[:, :], code[:, :], 0x00080008, 12, ALU.bitwise_and,
                                  ALU.logical_shift_left).then_inc(f["mag"], 1)
                dve.wait_ge(f["mag"], j * 2 + 2)
                dve.tensor_tensor(mag[:, :], mag[:, :], sgn[:, :], ALU.bitwise_or).then_inc(f["or"], 1)
                dve.wait_ge(f["or"], j + 1)

            def scaled(j, slot):
                dve.wait_ge(f["slot_ready"], j)
                val = mag[:, :].bitcast(F16).rearrange("p (w o) -> p o w", o=2)
                for o in range(2):
                    dve.scalar_tensor_tensor(out=wf[:, o, :], in0=val[:, o, :], scalar=16384.0, in1=scl[:, slot, :],
                                             op0=ALU.mult, op1=ALU.mult).then_inc(f["wf_ready"], 1)

            codes(0, 0, 32)
            scaled(0, 0)

            for h in range(H1):
                dve.wait_ge(s1_full, h + 1)
                link(dve.tensor_tensor(a1[:, h, :], bank[4 + h][:, 0:P], cst[:, C_DECAY + h * P:C_DECAY + (h + 1) * P],
                                       ALU.mult))
                link(dve.scalar_tensor_tensor(out=a1m[:, h, :], in0=a1[:, h, :], scalar=-1.0, in1=a1[:, h, :],
                                              op0=ALU.mult, op1=ALU.max))
                dve.tensor_scalar(a1m[:, h, :], a1m[:, h, :], 1.0, None, ALU.max).then_inc(a1_ready, 1)

            def o_rows(b):
                return o1[:, b, :, :].rearrange("p h e -> p (h e)")

            def group_rows(c, step):
                dve.wait_ge(gated, 2 * (c + 1))
                dve.wait_ge(rstd_ready[4], c + 1)
                if step == 1:
                    dve.wait_ge(g_step, BPC * (c + 1))
                for b in range(c * BPC, (c + 1) * BPC):
                    if step == 0:
                        dve.scalar_tensor_tensor(out=o_rows(b), in0=o_rows(b), scalar=mv[:, b, 0:1], in1=gate[:, b, :],
                                                 op0=ALU.subtract, op1=ALU.mult).then_inc(g_step, 1)
                    else:
                        dve.scalar_tensor_tensor(out=xn[:, b, :], in0=o_rows(b), scalar=rs[:, b:b + 1],
                                                 in1=shift[:, b, :], op0=ALU.mult, op1=ALU.add).then_inc(xn_ready[4], 1)

            for c in range(NC):
                dve.wait_ge(o1_done, (c + 1) * H1)
                norm_stats(4, c, o_rows, EPS_GN)
            group_rows(0, 0)
            group_rows(0, 1)
            group_rows(1, 0)
            xt_low(4, [0])
            group_rows(1, 1)
            xt_low(4, [1])
            for c in range(NC):
                for r in chunk_pairs(c):
                    dve.wait_ge(wo1_full, r + 1)
                    residual(r, bank[4 + r]).then_inc(wo1_done, 1)
                if c:
                    norm_rows(5, c - 1, x_rows)
                dve.wait_ge(wo1_done, (c + 1) * BPC // 2)
                norm_stats(5, c, x_rows, EPS_LN)
            xt_low(5, [0])
            norm_rows(5, 1, x_rows)
            xt_low(5, [1])

            for k in range(2):
                dve.memset(unread[:, 4 + k:5 + k], 0.0).then_inc(f["pair_free"], 1)

            with dve.Fori(0, JT1 // 2) as i:
                for u in range(8):
                    s = u // 4
                    if u % 4 == 0:
                        codes(i * 2 + s + 1, 1 - s, i * 32 + 32 * (s + 1))
                    if u % 4 == 1:
                        scaled(i * 2 + s + 1, 1 - s)
                    hidden_rows(f, i * 8 + u, u)
            for r in range(B // 2):
                dve.wait_ge(f["down_full"], r + 1)
                residual(r, bank[4 + r]).then_inc(f["down_done"], 1)

        @block.tensor
        def _(pe):
            def product3(out, a, b, start=True, stop=True, **kw):
                pe.matmul(out, a[0], b[0], start=start, stop=False, **kw)
                pe.matmul(out, a[1], b[0], start=False, stop=False, **kw)
                return pe.matmul(out, a[0], b[1], start=False, stop=stop, **kw)

            def w0_part(w, k, s=slice(0, D)):
                return w0h[:, w, k, s], w0l[:, w, k, s]

            def transposes(i, src, need, chunks=range(NC)):
                for j in range(chunks.start * KT, chunks.stop * KT):
                    c, e = divmod(j, KT)
                    pe.wait_ge(need[0], need[1](c))
                    for q in range(BPC):
                        mm = pe.transpose(bank[j][:, q * P:(q + 1) * P], src(c * BPC + q, e), ident)
                    mm.then_inc(xt_full[i], 1)

            def rows_product(full, base, w, pairs=range(B // 2)):
                for r in pairs:
                    for b in (2 * r, 2 * r + 1):
                        out = bank[base + r][:, (b % 2) * D:(b % 2 + 1) * D]
                        for k in range(KT):
                            mm = product3(out, (xth[:, k, toks(b)], xtl[:, k, toks(b)]), w(k),
                                          start=(k == 0), stop=(k == KT - 1))
                    mm.then_inc(full, 1)

            pe.wait_ge(wkv_lo, 1)
            for j in range(KT * NC):
                c, hd = divmod(j, KT)
                pe.wait_ge(ctx_lo, c + 1)
                for k in range(KT):
                    mm = product3(bank[j], w0_part(W_K, k, slice(hd * P, (hd + 1) * P)),
                                  (cth[:, k, cols(c)], ctl[:, k, cols(c)]), start=(k == 0), stop=(k == KT - 1))
                mm.then_inc(k_full, 1)

            def values(pairs):
                for r in pairs:
                    for b in (2 * r, 2 * r + 1):
                        for k in range(KT):
                            mm = product3(bank[4 + r][:, (b % 2) * D:(b % 2 + 1) * D],
                                          (cth[:, k, toks(b)], ctl[:, k, toks(b)]), w0_part(W_V, k),
                                          start=(k == 0), stop=(k == KT - 1))
                    mm.then_inc(v_full, 1)

            values(range(B // 4))
            pe.wait_ge(in_cst, 16)
            pe.wait_ge(k_lo, KT * NC)
            norm_out = lambda b, e: xn[:, b, e * P:(e + 1) * P]
            transposes(0, norm_out, (xn_ready[0], lambda c: BPC * (c + 1)), range(0, 1))
            values(range(B // 4, B // 2))
            transposes(0, norm_out, (xn_ready[0], lambda c: BPC * (c + 1)), range(1, NC))
            pe.wait_ge(w0_lo, 1)
            for j in range(KT * NC):
                c, hd = divmod(j, KT)
                pe.wait_ge(v_done, 2 * (j + 1))
                pe.wait_ge(xt_lo[0], KT * (c + 1))
                for k in range(KT):
                    mm = product3(bank[4 + j], w0_part(W_Q, k, slice(hd * P, (hd + 1) * P)),
                                  (xth[:, k, cols(c)], xtl[:, k, cols(c)]), start=(k == 0), stop=(k == KT - 1))
                mm.then_inc(q_full, 1)
            rows_product(g_full, 0, lambda k: w0_part(W_G, k))

            def scores(u):
                b, hd = divmod(u, KT)
                pe.wait_ge(km_ready, u + 1)
                if u >= 1:
                    pe.wait_ge(max_done, u)
                for j in range(2):
                    pe.matmul(bank[j], qh[:, hd, toks(b)], km[:, u % 2, 4 * j:4 * j + 4, :], start=True, stop=False)
                    mm = pe.matmul(bank[j], ones_r[:, :], maskr[:, toks(b)][:, None, :].broadcast_to([P, 4, P]),
                                   start=False, stop=True)
                mm.then_inc(s_full, 1)

            def scores_transposed(u):
                b, hd = divmod(u, KT)
                pe.wait_ge(qhm_ready, u + 1)
                pe.wait_ge(qlm_ready, HPT * (u + 1))
                pe.wait_ge(md_done, u + 1)
                if u >= 2:
                    pe.wait_ge(exp_done, u - 1)
                for j in range(2):
                    out, hs = bank[2 + 2 * (u % 2) + j], slice(4 * j, 4 * j + 4)
                    product3(out, (kh[:, hd, toks(b)], kl[:, hd, toks(b)]), (qhm[:, u % 2, hs, :], qlm[:, u % 2, hs, :]),
                             stop=False)
                    mm = pe.matmul(out, ones_r[:, :], mdiag[:, u % 2, hs, :], start=False, stop=True)
                mm.then_inc(st_full, 1)

            def group_means(i):
                pe.wait_ge(t_abs, i + 1)
                if i >= 1:
                    pe.wait_ge(t_scale, i)
                pe.matmul(bank[6], groupb[:, :], tab[:, i % 3, :], start=True, stop=True).then_inc(t_mean, 1)

            def weighted_values(u):
                b, hd = divmod(u, KT)
                pe.wait_ge(exp_done, u + 1)
                if hd == 0 and b >= 1:
                    pe.wait_ge(att_done, b)
                for h in range(HPT):
                    slot, j = divmod(hd * HPT + h, HB)
                    mm = pe.matmul(bank[7][j * HC:(j + 1) * HC, slot * P:(slot + 1) * P],
                                   vp[:, b, (hd * HPT + h) * (HD + 1):][:, 0:HC], pt[:, u % 2, h, :],
                                   start=True, stop=True)
                mm.then_inc(av_full, 1)

            def back_transpose(b):
                pe.wait_ge(av_copied, b + 1)
                for slot in range(NH // HB):
                    at = slice(slot * P, (slot + 1) * P)
                    mm = pe.transpose(bank[7][:, at], avt[:, at], ident)
                mm.then_inc(rows_full, 1)

            pe.wait_ge(g_done, B // 2)
            pe.wait_ge(q_lo, KT * NC)
            pe.wait_ge(masks_ready, B + 1)
            for u in range(-2, B * KT + 1):
                if u + 2 < B * KT:
                    scores(u + 2)
                if u >= 3 and u % 2 == 1:
                    back_transpose((u - 3) // 2)
                if 0 <= u < B * KT:
                    scores_transposed(u)
                if u == B * KT - 1:
                    pe.wait_ge(max_done, B * KT)
                    transposes(1, norm_out, (att_done, lambda c: BPC * (c + 1)), range(0, 1))
                if 0 <= u < TP:
                    group_means(u)
                if 0 <= u - 1:
                    weighted_values(u - 1)

            pe.wait_ge(exp_done, B * KT)
            pe.wait_ge(xt_lo[1], KT)
            rows_product(wo_full, 4, lambda k: w0_part(W_O, k), range(0, B // 4))
            back_transpose(B - 1)
            transposes(1, norm_out, (att_done, lambda c: BPC * (c + 1)), range(1, NC))
            pe.wait_ge(xt_lo[1], KT * NC)
            rows_product(wo_full, 4, lambda k: w0_part(W_O, k), range(B // 4, B // 2))

            pe.wait_ge(w1_lo, 1)
            for j in range(H1 * NC):
                h, c = divmod(j, NC)
                pe.matmul(bank[j], wh1(w1, h), ct[:, h, cols(c)], start=True, stop=True).then_inc(k1_full, 1)
            pe.wait_ge(k1_done, H1 * NC)
            transposes(2, norm_out, (xn_ready[2], lambda c: BPC * (c + 1)))

            def ffn(f, units, passes, weights, chunk_done=None):
                def gate_up(k, u):
                    c = u % 2
                    pe.wait_ge(f["pair_free"], k + 1)
                    for part, full in ((0, "gate_full"), (1, "up_full")):
                        for e in range(KT):
                            wts = weights(u, part, e)
                            last = e == KT - 1
                            out = bank[2 * c + part]
                            pe.matmul(out, wts[0], xth[:, e, cols(c)], start=(e == 0), stop=False)
                            mm = pe.matmul(out, wts[0], xtl[:, e, cols(c)], start=False,
                                           stop=last and passes == 2)
                            if passes == 3:
                                mm = pe.matmul(out, wts[1], xth[:, e, cols(c)], start=False, stop=last)
                        mm.then_inc(f[full], 1)

                def down(u, full=None):
                    c = u % 2
                    wts = weights(u, 2, 0)
                    for q in range(BPC):
                        b = c * BPC + q
                        out = bank[4 + b // 2][:, (b % 2) * D:(b % 2 + 1) * D]
                        hi, lo = hidh[:, c, toks(q)], hidl[:, c, toks(q)]
                        pe.matmul(out, hi, wts[0], start=False, stop=False, skip_group_check=True)
                        mm = pe.matmul(out, lo, wts[0], start=False, stop=False, skip_group_check=True)
                        if passes == 3:
                            mm = pe.matmul(out, hi, wts[1], start=False, stop=False, skip_group_check=True)
                    return mm

                tiles_per_slot = 1 if passes == 2 else 2
                n_loops = units[0]
                for r in range(B // 2):
                    pe.matmul(bank[4 + r], zero_r[:, :], xth[:, 0, 0:CH], start=True, stop=False, skip_group_check=True)
                with pe.Fori(0, n_loops) as i:
                    for u in range(units[1]):
                        k = i * units[1] + u
                        if u % (2 * tiles_per_slot) == 0:
                            pe.wait_ge(f["slot_ready"], i * 2 + u // (2 * tiles_per_slot) + 1)
                        gate_up(k, u)
                        pe.wait_ge(f["hid_ready"], k + 1)
                        down((u - 1) % units[1]).then_inc(f["down_turn"], 1)
                for c in range(NC):
                    if c:
                        pe.wait_ge(f["hid_ready"], n_loops * units[1] + 1)
                        down(units[1] - 1).then_inc(f["down_turn"], 1)
                    for r in range(c * BPC // 2, (c + 1) * BPC // 2):
                        pe.matmul(bank[4 + r], zero_r[:, :], xth[:, 0, 0:CH], start=False, stop=True,
                                  skip_group_check=True).then_inc(f["down_full"], 1)
                    if chunk_done:
                        chunk_done(c)

            def ternary(u, part, e):
                s = u // 2
                at = 2 * KT * P if part == 2 else (part * KT + e) * P
                return (slot0[:, s, at:at + (D if part == 2 else P)],)

            def unpacked(u, part, e):
                s, par = u // 4, u // 2 % 2
                if part == 2:
                    return slh[:, s, par, 4 * P:4 * P + D], sll[:, s, par, 4 * P:4 * P + D]
                at = (2 * par + part) * P
                return slh[:, s, e, at:at + P], sll[:, s, e, at:at + P]

            pe.wait_ge(xt_lo[2], KT * NC)
            pe.wait_ge(wo_done, B // 2)

            def mean_squares(c):
                pe.wait_ge(fs[0]["acc_done"], 2 * HT0 + 2 + c)
                pe.wait_ge(fs[0]["pair_free"], 2 * HT0 + 1 + c)
                for q in range(BPC):
                    mm = pe.matmul(bank[c][:, q:q + 1], acc[:, c, toks(q)], onesf[:, :], start=True, stop=True)
                mm.then_inc(ms_full, 1)

            ffn(fs[0], (HT0 // 2, 4), 2, ternary, mean_squares)

            for j in V1_ORDER:
                if j < NC:
                    pe.wait_ge(ms_scaled, j + 1)
                h, c = divmod(j, NC)
                for q in range(BPC):
                    mm = pe.matmul(bank[j][:, q * P:(q + 1) * P], ct[:, h, toks(c * BPC + q)], wh1(w1, h),
                                   start=True, stop=True)
                mm.then_inc(v1_full, 1)

            pe.wait_ge(v1_done, H1 * NC)
            for c in range(NC):
                transposes(3, norm_out, (xn_ready[3], lambda c: BPC * (c + 1)),
                           range(c, c + 1))
                pe.wait_ge(xt_lo[3], KT * (c + 1))
                rows_product(g1_full, 0, lambda k: (wg1(w1h, k), wg1(w1l, k)), range(c * BPC // 2, (c + 1) * BPC // 2))
                pe.wait_ge(fs[0]["down_done"], B)
                for h in range(H1):
                    product3(bank[4 + c * H1 + h], (wh1(w1h, h), wh1(w1l, h)), (xth[:, h, cols(c)], xtl[:, h, cols(c)])
                             ).then_inc(q1_full, 1)
            pe.wait_ge(q1_done, H1 * NC)
            for h in range(H1):
                for b in range(B):
                    mm = pe.matmul(bank[4 + h][:, 0:P], k1t[:, h, toks(b)], q1t[:, h, toks(b)],
                                   start=(b == 0), stop=(b == B - 1))
                mm.then_inc(s1_full, 1)
            pe.wait_ge(g1_done, B // 2)
            for j in range(H1 * NC):
                c, h = divmod(j, H1)
                pe.wait_ge(a1_ready, h + 1)
                pe.matmul(bank[j], a1m[:, h, :], v1[:, h, BPC * c:BPC * (c + 1), :], start=True,
                          stop=True).then_inc(o1_full, 1)
            for c in range(NC):
                transposes(4, norm_out, (xn_ready[4], lambda c: BPC * (c + 1)),
                           range(c, c + 1))
                pe.wait_ge(xt_lo[4], KT * (c + 1))
                rows_product(wo1_full, 4, lambda k: (wo1(w1h, k), wo1(w1l, k)),
                             range(c * BPC // 2, (c + 1) * BPC // 2))
            transposes(5, lambda b, e: xn[:, b, e:D:KT], (xn_ready[5], lambda c: BPC * (c + 1)))
            pe.wait_ge(xt_lo[5], KT * NC)
            pe.wait_ge(wo1_done, B // 2)
            ffn(fs[1], (JT1 // 2, 8), 3, unpacked)


def constants():
    s = np.arange(P, dtype=np.float64)
    table = np.zeros((P, C_END), np.float32)
    for h in range(H1):
        back = s[:, None] - s[None, :]
        gam = 1.0 - 2.0 ** (-5.0 - h)
        d = np.where(back >= 0, gam ** -np.maximum(back, 0.0), 0.0)
        d = d / np.sqrt(d.sum(-1))[None, :] / np.sqrt(P)
        table[:, C_DECAY + h * P:C_DECAY + (h + 1) * P] = d.T
    table[:, C_IDENT:C_IDENT + P] = np.eye(P)
    table[:, C_HEAD:C_HEAD + HPT] = np.arange(P)[:, None] // HD == np.arange(HPT)
    g = np.arange(P) // 64
    table[:, C_GROUP:C_GROUP + P] = (g[:, None] == g) / 64.0
    return table


def kernel(**inputs):
    import concourse.bacc as bacc
    from concourse.bass_utils import run_bass_kernel_spmd

    a = {k: np.asarray(v) for k, v in inputs.items()}
    con = np.ascontiguousarray

    def rows(w):
        return w.reshape(KT, P, -1).transpose(1, 0, 2)

    mask = a["mask_BxS2_bk0"]
    w0 = np.stack([rows(a[f"L0_xattn_{n}"].T) for n in ("wk", "wv", "wq", "wg", "wo")], 1)
    w1 = np.concatenate([rows(a["L1_xattn_wg_w"]).reshape(P, -1), rows(a["L1_xattn_wo_w"]).reshape(P, -1),
                         a["L1_xattn_Wh"].transpose(1, 0, 2).reshape(P, -1)], 1)
    gu = a["L0_ffn_w_gate_up"].reshape(2, HT0, P, KT, P)
    gu = gu.transpose(4, 1, 0, 3, 2).reshape(P, HT0, 2 * KT * P)
    down0 = a["L0_ffn_w_proj"].reshape(D, HT0, P).transpose(2, 1, 0)
    tern = np.concatenate([gu, down0], 2).reshape(P, -1)

    def pairs(w, width):
        return w.reshape(JT1, P, 2, width).transpose(3, 0, 2, 1)

    def joined(g, u, d):
        gu = np.stack([g, u], 3).reshape(g.shape[0], JT1, 4 * P)
        return np.concatenate([gu, d], 2)

    packed = joined(pairs(a["L1_ffn_gate_W_packed"], P), pairs(a["L1_ffn_up_W_packed"], P),
                    a["L1_ffn_down_W_packed"].reshape(D, JT1, P).transpose(2, 1, 0))
    scl = joined(pairs(a["L1_ffn_gate_scales"], 8), pairs(a["L1_ffn_up_scales"], 8),
                 a["L1_ffn_down_scales"].reshape(D, JT1, 8).transpose(2, 1, 0))

    arrays = {
        "x": a["x"], "ctx": rows(a["ctx_2048"].reshape(TOK, D).T), "w0": w0, "w1": w1, "tern": tern,
        "packed": packed, "scl": scl, "maskc": con(mask.T).view(np.int32), "maskr": con(mask.reshape(1, TOK)).view(np.int32),
        "normw": a["L0_xattn_norm_w"].reshape(KT, P).T, "gamma": a["L1_xattn_gn_gamma"].reshape(1, D),
        "beta": a["L1_xattn_gn_beta"].reshape(1, D), "cst": constants(),
    }
    nc = bacc.Bacc("TRN2", target_bir_lowering=False, num_devices=1)
    sent, t = {}, {}
    for name, v in arrays.items():
        v = con(v)
        sent[f"in_{name}"] = v
        t[name] = nc.dram_tensor(f"in_{name}", v.shape, mybir.dt.from_np(v.dtype), kind="ExternalInput").ap()
    t["x"] = t["x"].rearrange("b s d -> s b d")
    t["out"] = nc.dram_tensor("out", (B, P, D), F32, kind="ExternalOutput").ap().rearrange("b s d -> s b d")
    for name in ("gamma", "beta"):
        t[name] = t[name].broadcast_to([P, D])
    scales = t["scl"]
    t["scl"] = lambda pair: scales[:, None, pair, :].broadcast_to([8, P // 8, 1, WCOL])
    build(nc, t)
    r = run_bass_kernel_spmd(nc, [sent], core_ids=[0])
    return r.results[0]["out"]
```
